# Optimizing a Trainium2 kernel written in Bass

```python
import numpy as np
import jax
import jax.numpy as jnp

def _softmax(x, axis=-1):
    return jax.nn.softmax(x, axis=axis)

def _gelu(x):
    return jax.nn.gelu(x, approximate=True)

def _silu(x):
    return jax.nn.silu(x)

def _sigmoid(x):
    return jax.nn.sigmoid(x)

def _layernorm(x, axis=-1, eps=1e-05):
    m = jnp.mean(x, axis=axis, keepdims=True)
    v = jnp.var(x, axis=axis, keepdims=True)
    return (x - m) / jnp.sqrt(v + eps)

def _scatter_add(tgt, idx, src, axis=0):
    return tgt.at[idx].add(src)

def _segment_sum(src, seg, n):
    return jax.ops.segment_sum(src, seg, n)
kernel_name = 'mk_sandwich_d1_jaxref_r8_95e8ee'

def setup_inputs(seed: int=0):
    np.random.seed(seed)
    _w = jnp.asarray

    def _L0_attn_setup():
        import jax, jax.numpy as jnp
        import numpy as np
        B, S, H = (1, 256, 512)
        NH = 32
        Q_LORA, KV_LORA = (192, 64)
        QK_NOPE, QK_ROPE = (128, 64)
        Q_HEAD = QK_NOPE + QK_ROPE
        V_HEAD = 128
        key = jax.random.key(seed)
        ks = jax.random.split(key, 12)

        def lin(k, out_d, in_d):
            s = 1.0 / np.sqrt(in_d)
            return jax.random.uniform(k, (out_d, in_d), jnp.float32, -s, s)
        return {'hidden_size': jax.random.normal(ks[0], (B, S, H), jnp.float32), 'Wq_c': lin(ks[1], Q_LORA, H), 'bq_c': jnp.zeros((Q_LORA,), jnp.float32), 'Wq_up': lin(ks[2], NH * Q_HEAD, Q_LORA), 'bq_up': jnp.zeros((NH * Q_HEAD,), jnp.float32), 'Wkv_c': lin(ks[3], KV_LORA + QK_ROPE, H), 'bkv_c': jnp.zeros((KV_LORA + QK_ROPE,), jnp.float32), 'Wkv_up': lin(ks[4], NH * (QK_NOPE + V_HEAD), KV_LORA), 'bkv_up': jnp.zeros((NH * (QK_NOPE + V_HEAD),), jnp.float32), 'Wo': lin(ks[5], H, V_HEAD), 'bo': jnp.zeros((H,), jnp.float32)}
    _L0_attn_in = _L0_attn_setup()

    def _L0_ffn_setup():
        import jax, jax.numpy as jnp
        import numpy as np
        NF4_CODE = jnp.array([-1.0, -0.6961928009986877, -0.5250730514526367, -0.39491748809814453, -0.28444138169288635, -0.18477343022823334, -0.09105003625154495, 0.0, 0.07958029955625534, 0.16093020141124725, 0.24611230194568634, 0.33791524171829224, 0.44070982933044434, 0.5626170039176941, 0.7229568362236023, 1.0], dtype=jnp.float32)
        BLOCKSIZE = 64

        def nf4_quant_dequant(w):
            shape = w.shape
            flat = w.reshape(-1, BLOCKSIZE)
            absmax = jnp.max(jnp.abs(flat), axis=1, keepdims=True)
            normalized = flat / jnp.where(absmax == 0, 1.0, absmax)
            bounds = (NF4_CODE[:-1] + NF4_CODE[1:]) * 0.5
            idx = jnp.searchsorted(bounds, normalized)
            return (NF4_CODE[idx] * absmax).reshape(shape)
        key = jax.random.key(seed)
        k1, k2, k3, kx = jax.random.split(key, 4)
        D, H = (512, 1376)
        scale = 0.02
        w1 = jax.random.normal(k1, (H, D), jnp.float32) * scale
        w2 = jax.random.normal(k2, (H, D), jnp.float32) * scale
        w3 = jax.random.normal(k3, (D, H), jnp.float32) * scale
        x = jax.random.normal(kx, (2, 256, D), jnp.float32)
        return {'x': x, 'w1': w1, 'w2': w2, 'w3': w3}
    _L0_ffn_in = _L0_ffn_setup()
    _d = {'L0_attn_hidden_size': _L0_attn_in['hidden_size'], 'L0_attn_Wq_c': _L0_attn_in['Wq_c'], 'L0_attn_bq_c': _L0_attn_in['bq_c'], 'L0_attn_Wq_up': _L0_attn_in['Wq_up'], 'L0_attn_bq_up': _L0_attn_in['bq_up'], 'L0_attn_Wkv_c': _L0_attn_in['Wkv_c'], 'L0_attn_bkv_c': _L0_attn_in['bkv_c'], 'L0_attn_Wkv_up': _L0_attn_in['Wkv_up'], 'L0_attn_bkv_up': _L0_attn_in['bkv_up'], 'L0_attn_Wo': _L0_attn_in['Wo'], 'L0_attn_bo': _L0_attn_in['bo'], 'L0_ffn_w1': _L0_ffn_in['w1'], 'L0_ffn_w2': _L0_ffn_in['w2'], 'L0_ffn_w3': _L0_ffn_in['w3']}
    _x0 = _d['L0_attn_hidden_size']
    _d['L0_attn_hidden_size'] = jax.random.normal(jax.random.fold_in(jax.random.key(seed), 1), (4, 512, 512), dtype=_x0.dtype)
    del _x0
    return _d

def reference(L0_attn_hidden_size, L0_attn_Wq_c, L0_attn_bq_c, L0_attn_Wq_up, L0_attn_bq_up, L0_attn_Wkv_c, L0_attn_bkv_c, L0_attn_Wkv_up, L0_attn_bkv_up, L0_attn_Wo, L0_attn_bo, L0_ffn_w1, L0_ffn_w2, L0_ffn_w3):

    def _L0_attn_ref(hidden_size, Wq_c, bq_c, Wq_up, bq_up, Wkv_c, bkv_c, Wkv_up, bkv_up, Wo, bo):
        import jax, jax.numpy as jnp
        import numpy as np
        B, S, H = (1, 256, 512)
        NH = 32
        Q_LORA, KV_LORA = (192, 64)
        QK_NOPE, QK_ROPE = (128, 64)
        Q_HEAD = QK_NOPE + QK_ROPE
        V_HEAD = 128
        b, s, _ = hidden_size.shape
        q_c = hidden_size @ Wq_c.T + bq_c
        q = (q_c @ Wq_up.T + bq_up).reshape(b, s, NH, Q_HEAD).transpose(0, 2, 1, 3)
        kv = hidden_size @ Wkv_c.T + bkv_c
        kv_nope, kv_rope = (kv[..., :KV_LORA], kv[..., KV_LORA:])
        kvu = (kv_nope @ Wkv_up.T + bkv_up).reshape(b, s, NH, QK_NOPE + V_HEAD).transpose(0, 2, 1, 3)
        k_nope, v = (kvu[..., :QK_NOPE], kvu[..., QK_NOPE:])
        k_rope = jnp.broadcast_to(kv_rope[:, None, :, :], (b, NH, s, QK_ROPE))
        k = jnp.concatenate([k_nope, k_rope], axis=-1)
        scores = jnp.einsum('bhqd,bhkd->bhqk', q, k) / np.sqrt(Q_HEAD)
        attn = jax.nn.softmax(scores, axis=-1)
        o = jnp.einsum('bhqk,bhkv->bhqv', attn, v)
        out = jnp.einsum('bhsv,Hv->bsH', o, Wo) + bo
        return out

    def _L0_ffn_ref(x, w1, w2, w3):
        import jax, jax.numpy as jnp
        import numpy as np
        NF4_CODE = jnp.array([-1.0, -0.6961928009986877, -0.5250730514526367, -0.39491748809814453, -0.28444138169288635, -0.18477343022823334, -0.09105003625154495, 0.0, 0.07958029955625534, 0.16093020141124725, 0.24611230194568634, 0.33791524171829224, 0.44070982933044434, 0.5626170039176941, 0.7229568362236023, 1.0], dtype=jnp.float32)
        BLOCKSIZE = 64

        def nf4_quant_dequant(w):
            shape = w.shape
            flat = w.reshape(-1, BLOCKSIZE)
            absmax = jnp.max(jnp.abs(flat), axis=1, keepdims=True)
            normalized = flat / jnp.where(absmax == 0, 1.0, absmax)
            bounds = (NF4_CODE[:-1] + NF4_CODE[1:]) * 0.5
            idx = jnp.searchsorted(bounds, normalized)
            return (NF4_CODE[idx] * absmax).reshape(shape)
        dq1 = nf4_quant_dequant(w1)
        dq2 = nf4_quant_dequant(w2)
        dq3 = nf4_quant_dequant(w3)
        gate = jnp.einsum('bsd,hd->bsh', x, dq1)
        up = jnp.einsum('bsd,hd->bsh', x, dq2)
        h = jax.nn.silu(gate) * up
        return jnp.einsum('bsh,dh->bsd', h, dq3)
    x = L0_attn_hidden_size
    x = x + _layernorm(_L0_attn_ref(_layernorm(x, axis=-1), L0_attn_Wq_c, L0_attn_bq_c, L0_attn_Wq_up, L0_attn_bq_up, L0_attn_Wkv_c, L0_attn_bkv_c, L0_attn_Wkv_up, L0_attn_bkv_up, L0_attn_Wo, L0_attn_bo), axis=-1)
    x = x + _layernorm(_L0_ffn_ref(_layernorm(x, axis=-1), L0_ffn_w1, L0_ffn_w2, L0_ffn_w3), axis=-1)
    return x

_drawn_inputs = setup_inputs


def setup_inputs(seed=0):
    import zlib

    import numpy as np

    out = dict(_drawn_inputs(seed))
    spreads = {'L0_attn_bq_c': (0.0, 0.8),
     'L0_attn_bq_up': (0.0, 0.8),
     'L0_attn_bkv_c': (0.0, 0.1),
     'L0_attn_bkv_up': (0.0, 0.1),
     'L0_attn_bo': (0.0, 0.1)}
    factors = {}
    for name, (base, spread) in spreads.items():
        noise = np.random.default_rng([zlib.crc32(name.encode()), seed]).standard_normal(out[name].shape)
        drawn = base * np.exp(spread * noise) if base else spread * noise
        out[name] = jnp.asarray(drawn.astype(out[name].dtype))
    for name, factor in factors.items():
        out[name] = (out[name] * factor).astype(out[name].dtype)
    return out
```

```python
from contextlib import ExitStack

import numpy as np

import concourse.bass as bass
from concourse import mybir

F32 = mybir.dt.float32
F32R = mybir.dt.float32r
ALU = mybir.AluOpType
ACT = mybir.ActivationFunctionType
AX_X = mybir.AxisListType.X

P = 128
B, S, H = 4, 512, 512
TOK = B * S
NT = TOK // P
TB = S // P
HT = H // P
NH = 32
QL, C, ROPE, NOPE, VD = 192, 64, 64, 128, 128
PAIRS = NH // 2
NP = B * PAIRS
SCALE = 1.0 / float(np.sqrt(NOPE + ROPE))
EPS = 1e-5
F = 1376
FT = (F + P - 1) // P
FK = [P] * (FT - 1) + [F - (FT - 1) * P]
FP = FT * P
BLK = 64
W1_AT, W2_AT, W3_AT = 0, FT * H, 2 * FT * H
W3_Q = 4
CH = 256
NCH = -(-(W3_AT + W3_Q * F) // CH)
QCOLS = NCH * CH
LEAD = NCH - NP
assert LEAD == 2

_NF4 = np.array([-1.0, -0.6961928009986877, -0.5250730514526367, -0.39491748809814453, -0.28444138169288635,
                 -0.18477343022823334, -0.09105003625154495, 0.0, 0.07958029955625534, 0.16093020141124725,
                 0.24611230194568634, 0.33791524171829224, 0.44070982933044434, 0.5626170039176941,
                 0.7229568362236023, 1.0], dtype=np.float32)
BOUNDS = [float(v) for v in (_NF4[:-1] + _NF4[1:]) * np.float32(0.5)]
STEPS = [float(v) for v in _NF4[1:] - _NF4[:-1]]
LEVELS = len(BOUNDS)

SBUF_AT, SBUF_END = 16512, 229344


def after(engine, semaphore, value):
    if not (isinstance(value, int) and value <= 0):
        engine.wait_ge(semaphore, value)


def layout(nc):
    m = {}

    def put(at, items):
        for name, shape, dt in items:
            size = 4 * int(np.prod(shape[1:]))
            m[name] = nc.alloc_sbuf_tensor_at(name, shape, dt, offset=at)
            at += (size + 31) // 32 * 32
        assert at <= SBUF_END, (items[-1][0], at)
        return at

    shared = put(SBUF_AT, [
        ("ident", [P, P], F32), ("osum", [P, TOK], F32), ("bv_sum", [P, 1], F32),
    ])
    kept = put(shared, [
        ("m_all", [P, NH, 2, 2, P], F32R),
        ("q_bias", [P, NH], F32),
        ("kv_hi", [P, TOK], F32R), ("kv_lo", [P, TOK], F32R),
        ("qa_hi", [P, TOK], F32R), ("qa_lo", [P, TOK], F32R),
        ("qb", [P, TOK], F32R),
        ("c_nat", [P, B, TB, C], F32),
    ])
    quant = put(kept, [
        ("w_in", [P, 2, CH], F32), ("w_n", [P, CH], F32), ("w_step", [P, 2, CH], F32),
        ("w_acc", [P, CH], F32), ("w_out", [P, 2, CH], F32), ("w_max", [P, CH // BLK], F32),
        ("w_safe", [P, CH // BLK], F32), ("w_rcp", [P, CH // BLK], F32), ("minus1", [P, CH], F32),
    ])
    put(quant, [
        ("prob", [P, 8, S], F32), ("prob_t", [P, 2, 2, TB, S], F32),
        ("qe_hi", [P, 2, S], F32R), ("qe_lo", [P, 2, S], F32R),
        ("m_now", [P, 2, 2, 2, 2, P], F32R), ("wv_now", [P, 2, VD], F32), ("c_now", [P, 2, TB, C], F32),
        ("bias_now", [P, 2, 2], F32), ("ctx", [P, 2, S], F32),
        ("negmax", [P, 8], F32), ("rowsum", [P, 8], F32), ("rinv", [P, 8], F32),
    ])
    put(quant, [
        ("x_all", [P, NT, H], F32), ("x_norm", [P, TB, H], F32),
        ("xt_hi", [P, HT, S], F32R), ("xt_lo", [P, HT, S], F32R),
        ("wq_hi", [P, HT, 2 * P], F32R), ("wq_lo", [P, HT, 2 * P], F32R),
        ("wkv_hi", [P, HT, P], F32R), ("wkv_lo", [P, HT, P], F32R),
        ("kv_f", [P, S], F32), ("bqc", [P, 2], F32), ("bkvc", [P, 1], F32),
        ("bqn", [P, NH], F32), ("bqr", [P, NH], F32), ("bv", [P, NH], F32),
        ("wn_in", [P, 2, 2, 2 * P], F32), ("wk_in", [P, 2, 2, C], F32), ("wr_in", [P, 2, 2, 2, ROPE], F32),
        ("st1", [P, TB, 6], F32), ("mv1", [P, TB, 2], F32), ("sd1", [P, TB], F32), ("rs1", [P, TB], F32), ("eps1", [P, 1], F32), ("fence1", [P, 1], F32),
    ])
    put(shared, [
        ("w1_hi", [P, HT, FP], F32R), ("w1_lo", [P, HT, FP], F32R),
        ("w2_hi", [P, HT, FP], F32R), ("w2_lo", [P, HT, FP], F32R),
        ("w3_hi", [P, FT, H], F32R), ("w3_lo", [P, FT, H], F32R),
        ("dq_in", [P, 3, H], F32),
        ("x1t_hi", [P, HT, S], F32R), ("x1t_lo", [P, HT, S], F32R),
        ("x1", [P, TB, H], F32), ("xn", [P, TB, H], F32),
        ("gate", [P, S], F32), ("hid", [P, S], F32),
        ("h_hi", [P, 2, S], F32R), ("h_lo", [P, 2, S], F32R),
        ("wo", [P, H], F32), ("bo", [P, H], F32), ("o_now", [P, S], F32),
        ("st2", [P, TB, 6], F32), ("mv2", [P, TB, 2], F32), ("sd2", [P, TB], F32), ("rs2", [P, TB], F32), ("eps2", [P, 1], F32), ("fence2", [P, 1], F32),
    ])
    raw = m["x_norm"][:, :, :].rearrange("p t d -> p (t d)")
    m["wq"] = raw[:, 0:2 * HT * P].rearrange("p (k c) -> p k c", k=HT)
    m["wkv"] = raw[:, 2 * HT * P:3 * HT * P].rearrange("p (k c) -> p k c", k=HT)
    return m


def block_kernel(nc, x, wq_cT, bq_c, wkv_cT, bkv_c, wq_nope, wq_ropeT, bq_nope, bq_rope, wk_up, wv_upT, bv_up,
                 woT, bo, w_ffn, ident, out):
    with ExitStack() as ctx:
        m = layout(nc)
        banks = ctx.enter_context(nc.psum_tensor("banks", [P, 8, 512], F32))
        dq = nc.dram_tensor("dq", (P, QCOLS), F32, kind="Internal").ap()

        def sem(name):
            return ctx.enter_context(nc.semaphore(name))

        def bank(k):
            return banks[:, k, :]

        x_tiles = x.rearrange("(t p) d -> t p d", p=P)
        out_tiles = out.rearrange("(b t p) d -> p b t d", p=P, t=TB)
        x_batch = x.rearrange("(b t p) d -> p b t d", p=P, t=TB)

        consts_in, weights_in, x_in = sem("consts_in"), sem("weights_in"), sem("x_in")
        wsplit_hi, wsplit = sem("wsplit_hi"), sem("wsplit")
        ln_stat, ln_var, ln_std, ln_rcp, ln_done = (sem(n) for n in ("ln_stat", "ln_var", "ln_std", "ln_rcp", "ln_done"))
        xt_psum, xt_hi_done, xt_split = sem("xt_psum"), sem("xt_hi_done"), sem("xt_split")
        proj_psum, proj_hi, proj_split = sem("proj_psum"), sem("proj_hi"), sem("proj_split")
        kvf_done, ct_psum, c_done = sem("kvf_done"), sem("ct_psum"), sem("c_done")
        head_in = [sem(f"head_in{u}") for u in range(2)]
        mh_psum, mh_hi, mh_split = sem("mh_psum"), sem("mh_hi"), sem("mh_split")
        bvs_done, osum_zero, rope_bias = sem("bvs_done"), sem("osum_zero"), sem("rope_bias")
        chunk_in, chunk_out = ([sem(f"{n}{u}") for u in range(2)] for n in ("chunk_in", "chunk_out"))
        quant_step, chunk_done = sem("quant_step"), sem("chunk_done")
        m_loaded, c_loaded, wv_loaded = (
            [sem(f"{n}{u}") for u in range(2)] for n in ("m_loaded", "c_loaded", "wv_loaded"))
        q_psum, q_hi, q_split = sem("q_psum"), sem("q_hi"), sem("q_split")
        score_psum, max_done, exp_done, rcp_done, prob_done = (
            sem(n) for n in ("score_psum", "max_done", "exp_done", "rcp_done", "prob_done"))
        probt_psum, probt_done = sem("probt_psum"), sem("probt_done")
        ctx_psum, ctx_done, o_psum, o_added = sem("ctx_psum"), sem("ctx_done"), sem("o_psum"), sem("o_added")
        dq_in_sem, wt_psum, wt_hi, wt_split = sem("dq_in_sem"), sem("wt_psum"), sem("wt_hi"), sem("wt_split")
        ffn_consts, x1_in, o_now_done, y_psum, y_done = (
            sem(n) for n in ("ffn_consts", "x1_in", "o_now_done", "y_psum", "y_done"))
        st_done, var_done, std_done, inv_done, norm_done, x1_done, xn_done = (
            sem(n) for n in ("st_done", "var_done", "std_done", "inv_done", "norm_done", "x1_done", "xn_done"))
        x1t_psum, x1t_hi_done, x1t_split = sem("x1t_psum"), sem("x1t_hi_done"), sem("x1t_split")
        gate_psum, up_psum, silu_done, hid_done, h_hi_done, h_split = (
            sem(n) for n in ("gate_psum", "up_psum", "silu_done", "hid_done", "h_hi_done", "h_split"))
        down_psum, out_stat, out_done, stored = sem("down_psum"), sem("out_stat"), sem("out_done"), sem("stored")

        blk = ctx.enter_context(nc.Block())

        @blk.sync
        def _(sp):
            for a, b_ in ((m["ident"], ident), (m["bqc"], bq_c), (m["bkvc"], bkv_c), (m["bqn"], bq_nope),
                          (m["bv"], bv_up)):
                sp.dma_start(a[:, :], b_).then_inc(consts_in, 16)
            sp.dma_start(m["bqr"][C:P, :], bq_rope).then_inc(consts_in, 16)
            for b in range(B):
                if b >= 1:
                    sp.wait_ge(x_in, 16 * TB * b)
                for t in range(TB * b, TB * b + TB):
                    sp.dma_start(m["x_all"][:, t, :], x_tiles[t]).then_inc(x_in, 16)
                if b == 0:
                    sp.dma_start(m["wq"][:, :, :], wq_cT).then_inc(weights_in, 16)
                    sp.dma_start(m["wkv"][:, :, :], wkv_cT).then_inc(weights_in, 16)

            def load_chunk(n, u):
                sp.dma_start(m["w_in"][:, u, :], w_ffn[:, bass.ds(n * CH, CH)]).then_inc(chunk_in[u], 16)

            def store_chunk(n, u):
                sp.wait_ge(chunk_done, n + 1)
                sp.dma_start(dq[:, bass.ds(n * CH, CH)], m["w_out"][:, u, :]).then_inc(chunk_out[u], 16)

            for n in range(2):
                load_chunk(n, n)

            def load_heads(p, u):
                sp.dma_start(m["wn_in"][:, u, :, :], wq_nope[:, bass.ds(2 * p, 2), :]).then_inc(head_in[u], 16)
                sp.dma_start(m["wk_in"][:, u, :, :], wk_up[:, bass.ds(2 * p, 2), :]).then_inc(head_in[u], 16)
                sp.dma_start(m["wr_in"][:, u, :, :, :], wq_ropeT[:, bass.ds(2 * p, 2), :, :]).then_inc(head_in[u], 16)

            for u in range(2):
                load_heads(u, u)
            def part(i):
                for u in range(2):
                    after(sp, mh_split, 2 * i + u + 1)
                    load_heads(2 * i + 2 + u, u)

            part(0)
            with sp.Fori(1, PAIRS // 2 - 1) as i:
                part(i)

            def load_m(n, u, first=False):
                if not first:
                    sp.wait_ge(q_split, 2 * n - 2)
                g = n % PAIRS
                sp.dma_start(m["m_now"][:, u, :, :, :, :].bitcast(F32),
                             m["m_all"][:, bass.ds(2 * g, 2), :, :, :].bitcast(F32)).then_inc(m_loaded[u], 16)
                sp.dma_start(m["bias_now"][:, u, :], m["q_bias"][:, bass.ds(2 * g, 2)]).then_inc(m_loaded[u], 16)

            def load_c(n, u, first=False):
                if not first:
                    sp.wait_ge(ctx_psum, n - 1)
                sp.dma_start(m["c_now"][:, u, :, :], m["c_nat"][:, bass.ds(n // PAIRS, 1), :, :]).then_inc(c_loaded[u], 16)
                if not first:
                    sp.wait_ge(o_psum, n - 1)
                sp.dma_start(m["wv_now"][:, u, :], wv_upT[:, bass.ds((n % PAIRS) * VD, VD)]).then_inc(wv_loaded[u], 16)

            sp.wait_ge(mh_split, PAIRS)
            sp.wait_ge(rope_bias, 1)
            sp.wait_ge(c_done, B)
            load_m(0, 0, True)
            for n in range(LEAD):
                store_chunk(n, n % 2)
                load_chunk(n + 2, n % 2)

            def step(n, u, first=False, last=False):
                if not last:
                    load_m(n + 1, 1 - u, first and u == 0)
                load_c(n, u, first)
                if not (first and u == 0):
                    store_chunk(n + LEAD - 1, 1 - u)
                    if not last:
                        load_chunk(n + LEAD + 1, 1 - u)

            for n in range(2):
                step(n, n, first=True)
            with sp.Fori(1, NP // 2 - 1) as i:
                for u in range(2):
                    step(2 * i + u, u)
            step(NP - 2, 0)
            step(NP - 1, 1, last=True)
            store_chunk(NCH - 1, 1)

            for u in range(2):
                sp.wait_ge(chunk_out[u], 8 * NCH)
            sp.wait_ge(o_added, NP)
            sp.dma_start(m["wo"][:, :], woT).then_inc(ffn_consts, 16)
            sp.dma_start(m["bo"][:, :], bo.partition_broadcast(P)).then_inc(ffn_consts, 16)

            def load_dq(i):
                for k, at in ((0, W1_AT), (1, W2_AT)):
                    sp.dma_start(m["dq_in"][:, k, :], dq[:, bass.ds(at + i * H, H)]).then_inc(dq_in_sem, 16)
                for q in range(W3_Q):
                    sp.dma_start(m["dq_in"][:, 2, q * P:(q + 1) * P],
                                 dq[:, bass.ds(W3_AT + q * F + i * P, P)]).then_inc(dq_in_sem, 16)

            def part(i):
                after(sp, wt_psum, 3 * i)
                load_dq(i)

            part(0)
            with sp.Fori(1, FT) as i:
                part(i)
            def part(b):
                after(sp, stored, 16 * b)
                sp.dma_start(m["x1"][:, :, :], x_batch[:, bass.ds(b, 1), :, :]).then_inc(x1_in, 16)
                after(sp, out_done, TB * (b + 1))
                sp.dma_start(out_tiles[:, bass.ds(b, 1), :, :], m["x1"][:, :, :]).then_inc(stored, 16)

            part(0)
            with sp.Fori(1, B) as b:
                part(b)
            sp.wait_ge(stored, 16 * B)

        @blk.tensor
        def _(pe):
            def three(o, lhs, rhs, first=True, last=True):
                pe.matmul(o, lhs[0], rhs[1], start=first, stop=False)
                pe.matmul(o, lhs[1], rhs[0], start=False, stop=False)
                return pe.matmul(o, lhs[0], rhs[0], start=False, stop=last)


            pe.wait_ge(consts_in, 96)
            pe.wait_ge(wsplit, 2)
            def part(b):
                for t in range(TB):
                    after(pe, ln_done, TB * b + t + 1)
                    after(pe, xt_split, TB * b + max(0, t - 1))
                    for k in range(HT):
                        last = pe.transpose(bank(t % 2)[:, k * P:(k + 1) * P],
                                            m["x_norm"][:, t, k * P:(k + 1) * P], m["ident"][:, :])
                    last.then_inc(xt_psum, 1)
                after(pe, xt_split, TB * b + TB)
                after(pe, proj_split, 3 * b)
                blocks = [(m["wkv_hi"], m["wkv_lo"], 0), (m["wq_hi"], m["wq_lo"], 0), (m["wq_hi"], m["wq_lo"], P)]
                for j, (hi, lo, at) in enumerate(blocks):
                    for k in range(HT):
                        last = three(bank(2 + j), (hi[:, k, at:at + P], lo[:, k, at:at + P]),
                                     (m["xt_hi"][:, k, :], m["xt_lo"][:, k, :]), k == 0, k == HT - 1)
                    last.then_inc(proj_psum, 1)
                after(pe, kvf_done, b + 1)
                after(pe, c_done, b)
                for t in range(TB):
                    last = pe.transpose(bank(5)[:, t * P:(t + 1) * P], m["kv_f"][:, t * P:(t + 1) * P],
                                        m["ident"][:, :])
                last.then_inc(ct_psum, 1)

            part(0)
            with pe.Fori(1, B) as b:
                part(b)

            def part(i):
                for u in range(2):
                    p = 2 * i + u
                    after(pe, head_in[u], 48 * i + 48)
                    after(pe, mh_split, 2 * i)
                    for h in range(2):
                        for ab in range(2):
                            pe.matmul(bank(6 + u)[:, (2 * h + ab) * C:(2 * h + ab + 1) * C],
                                      m["wn_in"][:, u, h, ab * P:(ab + 1) * P], m["wk_in"][:, u, h, :],
                                      start=True, stop=True)
                        last = pe.matmul(bank(6 + u)[0:C, 4 * C + h:4 * C + h + 1], m["wk_in"][:, u, h, :],
                                         m["bqn"][:, bass.ds(2 * p + h, 1)], start=True, stop=True)
                    last.then_inc(mh_psum, 1)

            part(0)
            with pe.Fori(1, PAIRS // 2) as i:
                part(i)

            def queries(n, s, u):
                j = 2 * n + s
                if s == 0:
                    pe.wait_ge(m_loaded[u], 16 * (n - u) + 32)
                if not (isinstance(j, int) and j == 0):
                    pe.wait_ge(q_split, j)
                tok = bass.ds((n // PAIRS) * S, S)
                w = m["m_now"]
                pe.matmul(bank(6), w[:, u, s, 0, 0, :], m["qa_lo"][:, tok], start=True, stop=False)
                pe.matmul(bank(6), w[:, u, s, 0, 1, :], m["qa_hi"][:, tok], start=False, stop=False)
                pe.matmul(bank(6), w[:, u, s, 1, 1, :], m["qb"][:, tok], start=False, stop=False)
                pe.matmul(bank(6), w[:, u, s, 1, 0, :], m["qb"][:, tok], start=False, stop=False)
                pe.matmul(bank(6), w[:, u, s, 0, 0, :], m["qa_hi"][:, tok], start=False, stop=True).then_inc(q_psum, 1)

            def transposes(k, tau):
                pe.wait_ge(prob_done, k + 1)
                if not (isinstance(k, int) and k < 2):
                    pe.wait_ge(probt_done, k - 1)
                for j in range(TB):
                    last = pe.transpose(bank(4 + tau % 2)[:, j * P:(j + 1) * P],
                                        m["prob"][:, tau, j * P:(j + 1) * P], m["ident"][:, :])
                last.then_inc(probt_psum, 1)

            def attend(n, u):
                pe.wait_ge(probt_done, 8 * n + 8)
                pe.wait_ge(c_loaded[u], 8 * (n - u) + 16)
                if not (isinstance(n, int) and n == 0):
                    pe.wait_ge(ctx_done, n)
                for j in range(TB):
                    for s in range(2):
                        last = pe.matmul(bank(7)[s * C:(s + 1) * C, :], m["c_now"][:, u, j, :],
                                         m["prob_t"][:, u, s, j, :], start=(j == 0), stop=(j == TB - 1))
                last.then_inc(ctx_psum, 1)

            def values(n, u):
                pe.wait_ge(ctx_done, n + 1)
                pe.wait_ge(wv_loaded[u], 8 * (n - u) + 16)
                pe.matmul(bank(6), m["wv_now"][:, u, :], m["ctx"][:, u, :], start=True, stop=True).then_inc(o_psum, 1)

            def step(n, u, first=False, last=False):
                for tau in range(8):
                    s, t = tau // 4, tau % 4
                    k = 8 * n + tau
                    if t == 0:
                        pe.wait_ge(q_split, 2 * n + s + 1)
                    if not (isinstance(k, int) and k < 4):
                        pe.wait_ge(exp_done, k - 3)
                    tok = bass.ds((n // PAIRS) * S, S)
                    three(bank(t), (m["qe_hi"][:, s, t * P:(t + 1) * P], m["qe_lo"][:, s, t * P:(t + 1) * P]),
                          (m["kv_hi"][:, tok], m["kv_lo"][:, tok])).then_inc(score_psum, 1)
                    if not (first and tau < 4):
                        transposes(k - 4, (tau + 4) % 8)
                    if tau == 0:
                        if not (isinstance(n, int) and n < 2):
                            pe.wait_ge(o_added, n - 1)
                        queries(n, 1, u)
                    if tau == 4 and not last:
                        queries(n + 1, 0, 1 - u)
                    if tau == 5 and not first:
                        attend(n - 1, 1 - u)
                    if tau == 7 and not first:
                        pe.wait_ge(q_split, 2 * n + (2 if last else 3))
                        values(n - 1, 1 - u)

            pe.wait_ge(proj_split, 3 * B)
            pe.wait_ge(c_done, B)
            pe.wait_ge(mh_split, PAIRS)
            queries(0, 0, 0)
            step(0, 0, first=True)
            step(1, 1)
            with pe.Fori(1, NP // 2 - 1) as i:
                for u in range(2):
                    step(2 * i + u, u)
            step(NP - 2, 0)
            step(NP - 1, 1, last=True)
            for tau in range(4, 8):
                transposes(8 * (NP - 1) + tau, tau)
            attend(NP - 1, 1)
            pe.wait_ge(o_added, NP - 1)
            values(NP - 1, 1)

            def part(i):
                after(pe, dq_in_sem, 96 * i + 96)
                for w in range(3):
                    after(pe, wt_split, 3 * i)
                    for k in range(4):
                        last = pe.transpose(bank(w)[:, k * P:(k + 1) * P],
                                            m["dq_in"][:, w, k * P:(k + 1) * P], m["ident"][:, :])
                    last.then_inc(wt_psum, 1)

            part(0)
            with pe.Fori(1, FT) as i:
                part(i)

            pe.wait_ge(wt_split, 3 * FT)
            pe.wait_ge(ffn_consts, 32)
            def part(b):
                after(pe, o_now_done, b + 1)
                after(pe, out_done, TB * b)
                for t in range(TB):
                    pe.matmul(bank(4 + t), m["o_now"][:, t * P:(t + 1) * P], m["wo"][:, :],
                              start=True, stop=True).then_inc(y_psum, 1)
                after(pe, hid_done, FT * b)
                for t in range(TB):
                    after(pe, xn_done, TB * b + t + 1)
                    for k in range(HT):
                        last = pe.transpose(bank(t)[:, k * P:(k + 1) * P], m["xn"][:, t, k * P:(k + 1) * P],
                                            m["ident"][:, :])
                    last.then_inc(x1t_psum, 1)
                after(pe, x1t_split, TB * b + TB)

                def up_and_gate(i):
                    after(pe, hid_done, FT * b + max(0, i - 1))
                    for at, hi, lo, done in ((0, m["w1_hi"], m["w1_lo"], gate_psum), (2, m["w2_hi"], m["w2_lo"], up_psum)):
                        for k in range(HT):
                            last = three(bank(at + i % 2), (hi[:, k, i * P:(i + 1) * P], lo[:, k, i * P:(i + 1) * P]),
                                         (m["x1t_hi"][:, k, :], m["x1t_lo"][:, k, :]), k == 0, k == HT - 1)
                        last.then_inc(done, 1)

                def down(i):
                    after(pe, h_split, FT * b + i + 1)
                    rows = FK[i]
                    for t in range(TB):
                        last = three(bank(4 + t), (m["h_hi"][0:rows, i % 2, t * P:(t + 1) * P],
                                                   m["h_lo"][0:rows, i % 2, t * P:(t + 1) * P]),
                                     (m["w3_hi"][0:rows, i, :], m["w3_lo"][0:rows, i, :]), i == 0, i == FT - 1)
                    last.then_inc(down_psum, 1)

                for i in range(FT):
                    up_and_gate(i)
                    if i >= 1:
                        down(i - 1)
                down(FT - 1)

            part(0)
            with pe.Fori(1, B) as b:
                part(b)

        @blk.scalar
        def _(act):
            def split_hi(o, i, **kw):
                return act.activation(o, i, ACT.Identity if "bias" in kw else ACT.Copy, **kw)

            act.wait_ge(weights_in, 32)
            split_hi(m["wkv_hi"][:, :, :], m["wkv"][:, :, :]).then_inc(wsplit_hi, 1)
            split_hi(m["wq_hi"][:, :, :], m["wq"][:, :, :]).then_inc(wsplit_hi, 1)
            act.wait_ge(consts_in, 96)
            def part(b):
                after(act, ln_var, TB * b + TB)
                act.activation(m["sd1"][:, :], m["mv1"][:, :, 1], ACT.Sqrt, bias=m["eps1"][:, 0:1]).then_inc(ln_std, 1)
                after(act, proj_psum, 3 * b)
                for t in range(TB):
                    after(act, xt_psum, TB * b + t + 1)
                    split_hi(m["xt_hi"][:, :, t * P:(t + 1) * P],
                             bank(t % 2).rearrange("p (k q) -> p k q", k=HT)).then_inc(xt_hi_done, 1)
                tok = bass.ds(b * S, S)
                for j, (hi, bias) in enumerate(((m["kv_hi"], m["bkvc"][:, 0:1]), (m["qa_hi"], m["bqc"][:, 0:1]),
                                                (m["qb"], m["bqc"][:, 1:2]))):
                    after(act, proj_psum, 3 * b + j + 1)
                    split_hi(hi[:, tok], bank(2 + j), bias=bias).then_inc(proj_hi, 1)
                after(act, ct_psum, b + 1)
                act.activation(m["c_nat"][:, bass.ds(b, 1), :, :],
                               bank(5).rearrange("p (a t q) -> p a t q", a=1, t=TB)[:, :, :, 0:C],
                               ACT.Copy).then_inc(c_done, 1)

            part(0)
            with act.Fori(1, B) as b:
                part(b)
            def part(i):
                for u in range(2):
                    p = 2 * i + u
                    after(act, mh_psum, p + 1)
                    dst = m["m_all"][:, bass.ds(2 * p, 2), :, :, :].rearrange("p h a k c -> p (h a) k c")
                    act.activation(dst[:, :, 0, 0:C], bank(6 + u)[:, 0:4 * C].rearrange("p (a c) -> p a c", a=4),
                                   ACT.Copy, scale=SCALE).then_inc(mh_hi, 1)
                    act.activation(dst[:, :, 0, C:P], m["wr_in"][:, u, :, :, :].rearrange("p h a c -> p (h a) c"),
                                   ACT.Copy, scale=SCALE).then_inc(mh_hi, 1)
                    act.activation(m["q_bias"][0:C, bass.ds(2 * p, 2)], bank(6 + u)[0:C, 4 * C:4 * C + 2],
                                   ACT.Copy, scale=SCALE).then_inc(mh_hi, 1)

            part(0)
            with act.Fori(1, PAIRS // 2) as i:
                part(i)
            act.activation(m["q_bias"][C:P, :], m["bqr"][C:P, :], ACT.Copy, scale=SCALE).then_inc(rope_bias, 1)

            def queries_hi(j, s, u):
                act.wait_ge(q_psum, j + 1)
                if not (isinstance(j, int) and j < 2):
                    act.wait_ge(score_psum, 4 * j - 4)
                split_hi(m["qe_hi"][:, s, :], bank(6), bias=m["bias_now"][:, u, s:s + 1]).then_inc(q_hi, 1)

            def evacuate(n, tau, u):
                act.wait_ge(probt_psum, 8 * n + tau + 1)
                if tau == 0 and not (isinstance(n, int) and n < 2):
                    act.wait_ge(ctx_psum, n - 1)
                s, t = tau // 4, tau % 4
                act.activation(m["prob_t"][:, u, s, :, t * P:(t + 1) * P],
                               bank(4 + tau % 2).rearrange("p (j q) -> p j q", j=TB), ACT.Copy).then_inc(probt_done, 1)

            def step(n, u, first=False, last=False):
                for tau in range(8):
                    k = 8 * n + tau
                    if not (first and tau < 4):
                        evacuate(*((n, tau - 4, u) if tau >= 4 else (n - 1, tau + 4, 1 - u)))
                    act.wait_ge(max_done, k + 1)
                    if not first:
                        act.wait_ge(probt_psum, k - 7)
                    act.activation(m["prob"][:, tau, :], bank(tau % 4), ACT.Exp, bias=m["negmax"][:, tau:tau + 1],
                                   accum_out=m["rowsum"][:, tau:tau + 1]).then_inc(exp_done, 1)
                    if tau == 0:
                        queries_hi(2 * n + 1, 1, u)
                    if tau == 4 and not last:
                        queries_hi(2 * n + 2, 0, 1 - u)
                    if tau == 6 and not first:
                        context(n - 1, 1 - u)

            def context(n, u):
                act.wait_ge(ctx_psum, n + 1)
                act.activation(m["ctx"][:, u, :], bank(7), ACT.Copy).then_inc(ctx_done, 1)

            act.wait_ge(mh_split, PAIRS)
            act.wait_ge(proj_split, 3 * B)
            queries_hi(0, 0, 0)
            step(0, 0, first=True)
            step(1, 1)
            with act.Fori(1, NP // 2 - 1) as i:
                for u in range(2):
                    step(2 * i + u, u)
            step(NP - 2, 0)
            step(NP - 1, 1, last=True)
            for tau in range(4, 8):
                evacuate(NP - 1, tau, 1)
            context(NP - 1, 1)

            act.wait_ge(o_added, NP)
            for u in range(2):
                act.wait_ge(chunk_out[u], 8 * NCH)
            def part(i):
                for w, hi in ((0, m["w1_hi"]), (1, m["w2_hi"])):
                    after(act, wt_psum, 3 * i + w + 1)
                    split_hi(hi[:, :, bass.ds(i * P, P)], bank(w).rearrange("p (k q) -> p k q", k=HT)).then_inc(wt_hi, 1)
                after(act, wt_psum, 3 * i + 3)
                split_hi(m["w3_hi"][:, bass.ds(i, 1), :].rearrange("p a (t q r) -> p (a t) r q", t=2, r=2),
                         bank(2).rearrange("p (t r q) -> p t r q", t=2, r=2)).then_inc(wt_hi, 1)

            part(0)
            with act.Fori(1, FT) as i:
                part(i)
            act.wait_ge(bvs_done, 1)
            def part(b):
                after(act, y_psum, TB * b)
                act.activation(m["o_now"][:, :], m["osum"][:, bass.ds(b * S, S)], ACT.Identity,
                               bias=m["bv_sum"][:, 0:1]).then_inc(o_now_done, 1)
                for ln in range(2):
                    after(act, var_done, 3 * b + ln + 1)
                    act.activation(m["sd2"][:, :], m["mv2"][:, :, 1], ACT.Sqrt, bias=m["eps2"][:, 0:1]).then_inc(std_done, 1)
                for t in range(TB):
                    after(act, x1t_psum, TB * b + t + 1)
                    split_hi(m["x1t_hi"][:, :, t * P:(t + 1) * P],
                             bank(t).rearrange("p (k q) -> p k q", k=HT)).then_inc(x1t_hi_done, 1)

                def silu(i):
                    after(act, gate_psum, FT * b + i + 1)
                    after(act, hid_done, FT * b + i)
                    act.activation(m["gate"][:, :], bank(i % 2), ACT.Silu).then_inc(silu_done, 1)

                def hidden_hi(i):
                    after(act, hid_done, FT * b + i + 1)
                    if i >= 2:
                        after(act, down_psum, FT * b + i - 1)
                    split_hi(m["h_hi"][:, i % 2, :], m["hid"][:, :]).then_inc(h_hi_done, 1)

                for i in range(FT):
                    silu(i)
                    hidden_hi(i)
                after(act, var_done, 3 * b + 3)
                act.activation(m["sd2"][:, :], m["mv2"][:, :, 1], ACT.Sqrt, bias=m["eps2"][:, 0:1]).then_inc(std_done, 1)

            part(0)
            with act.Fori(1, B) as b:
                part(b)

        @blk.vector
        def _(dve):
            def f32(ap):
                return ap.bitcast(F32)

            def split_lo(o, full, hi):
                return dve.tensor_tensor(o, full, f32(hi), ALU.subtract)

            def levels(n, which):
                for lv in which:
                    base = n * (2 * LEVELS + 4) + 4 + 2 * lv
                    if lv >= 1:
                        dve.wait_ge(quant_step, base - 2)
                    dve.tensor_scalar(m["w_step"][:, lv % 2, :], m["w_n"][:, :], BOUNDS[lv], STEPS[lv],
                                      ALU.is_gt, ALU.mult).then_inc(quant_step, 1)
                    dve.wait_ge(quant_step, base + 1)
                    dve.tensor_tensor(m["w_acc"][:, :], m["w_step"][:, lv % 2, :],
                                      m["minus1"][:, :] if lv == 0 else m["w_acc"][:, :], ALU.add).then_inc(quant_step, 1)

            def blocks(ap):
                return ap.rearrange("p (k e) -> p k e", e=BLK)

            def quant_begin(n, u):
                base = n * (2 * LEVELS + 4)
                dve.wait_ge(chunk_in[u], 8 * (n - u) + 16)
                if not (isinstance(n, int) and n == 0):
                    dve.wait_ge(quant_step, base)
                    dve.wait_ge(chunk_done, n)
                w = m["w_in"][:, u, :]
                dve.tensor_reduce(m["w_max"][:, :], blocks(w), AX_X, ALU.max, apply_absolute_value=True).then_inc(quant_step, 1)
                dve.wait_ge(quant_step, base + 1)
                dve.scalar_tensor_tensor(out=m["w_safe"][:, :], in0=m["w_max"][:, :], scalar=0.0, in1=m["w_max"][:, :],
                                         op0=ALU.is_equal, op1=ALU.add).then_inc(quant_step, 1)
                dve.wait_ge(quant_step, base + 2)
                dve.reciprocal(m["w_rcp"][:, :], m["w_safe"][:, :]).then_inc(quant_step, 1)
                dve.wait_ge(quant_step, base + 3)
                dve.tensor_tensor(blocks(m["w_n"][:, :]), blocks(w),
                                  m["w_rcp"][:, :].unsqueeze(2).to_broadcast((P, CH // BLK, BLK)),
                                  ALU.mult).then_inc(quant_step, 1)
                dve.wait_ge(quant_step, base + 4)

            def quant_end(n, u):
                base = n * (2 * LEVELS + 4)
                dve.wait_ge(quant_step, base + 2 * LEVELS + 4)
                if not (isinstance(n, int) and n < 2):
                    dve.wait_ge(chunk_out[u], 8 * (n - u))
                dve.tensor_tensor(blocks(m["w_out"][:, u, :]), blocks(m["w_acc"][:, :]),
                                  m["w_max"][:, :].unsqueeze(2).to_broadcast((P, CH // BLK, BLK)),
                                  ALU.mult).then_inc(chunk_done, 1)

            dve.memset(m["eps1"][:, :], EPS).then_inc(osum_zero, 1)
            dve.memset(m["osum"][:, :], 0.0).then_inc(osum_zero, 1)
            dve.memset(m["minus1"][:, :], float(_NF4[0])).then_inc(osum_zero, 1)
            dve.wait_ge(consts_in, 96)
            dve.tensor_reduce(m["bv_sum"][:, :], m["bv"][:, :], AX_X, ALU.add).then_inc(bvs_done, 1)
            for k, (f, hi, lo) in enumerate((("wkv", "wkv_hi", "wkv_lo"), ("wq", "wq_hi", "wq_lo"))):
                dve.wait_ge(wsplit_hi, k + 1)
                split_lo(m[lo][:, :, :], m[f][:, :, :], m[hi][:, :, :]).then_inc(wsplit, 1)

            dve.wait_ge(wsplit, 2)
            def part(b):
                after(dve, x_in, 16 * TB * b + 16 * TB)
                after(dve, ln_done, TB * b)
                for t in range(TB):
                    dve.bn_stats(m["st1"][:, t, :], m["x_all"][:, bass.ds(TB * b + t, 1), :].rearrange("p a d -> p (a d)")).then_inc(ln_stat, 1)
                after(dve, ln_stat, TB * b + TB)
                dve.memset(m["fence1"][:, :], 0.0)
                for t in range(TB):
                    dve.bn_aggr(m["mv1"][:, t, :], m["st1"][:, t, :]).then_inc(ln_var, 1)
                after(dve, ln_std, b + 1)
                dve.reciprocal(m["rs1"][:, :], m["sd1"][:, :]).then_inc(ln_rcp, 1)
                after(dve, ln_rcp, b + 1)
                after(dve, xt_psum, TB * b)
                for t in range(TB):
                    dve.tensor_scalar(m["x_norm"][:, t, :], m["x_all"][:, bass.ds(TB * b + t, 1), :].rearrange("p a d -> p (a d)"),
                                      m["mv1"][:, t, 0:1], m["rs1"][:, t:t + 1], ALU.subtract, ALU.mult).then_inc(ln_done, 1)
                for t in range(TB):
                    after(dve, xt_hi_done, TB * b + t + 1)
                    split_lo(m["xt_lo"][:, :, t * P:(t + 1) * P], bank(t % 2).rearrange("p (k q) -> p k q", k=HT),
                             m["xt_hi"][:, :, t * P:(t + 1) * P]).then_inc(xt_split, 1)
                tok = bass.ds(b * S, S)
                after(dve, proj_hi, 3 * b + 1)
                after(dve, ct_psum, b)
                dve.tensor_scalar(m["kv_f"][:, :], bank(2), m["bkvc"][:, 0:1], None, ALU.add).then_inc(kvf_done, 1)
                for j, (lo, hi, bias, r) in enumerate(((m["kv_lo"], m["kv_hi"], m["bkvc"][:, 0:1], 0),
                                                       (m["qa_lo"], m["qa_hi"], m["bqc"][:, 0:1], 0),
                                                       (m["qb"], m["qb"], m["bqc"][:, 1:2], C))):
                    after(dve, proj_hi, 3 * b + j + 1)
                    dve.scalar_tensor_tensor(out=lo[r:P, tok], in0=bank(2 + j)[r:P, :], scalar=bias[r:P, :],
                                             in1=f32(hi[r:P, tok]), op0=ALU.add, op1=ALU.subtract).then_inc(proj_split, 1)

            part(0)
            with dve.Fori(1, B) as b:
                part(b)
            def part(i):
                for u in range(2):
                    p = 2 * i + u
                    after(dve, mh_hi, 3 * p + 3)
                    dst = m["m_all"][:, bass.ds(2 * p, 2), :, :, :].rearrange("p h a k c -> p (h a) k c")
                    dve.scalar_tensor_tensor(out=dst[:, :, 1, C:P], in0=m["wr_in"][:, u, :, :, :].rearrange("p h a c -> p (h a) c"),
                                             scalar=SCALE, in1=f32(dst[:, :, 0, C:P]), op0=ALU.mult, op1=ALU.subtract)
                    dve.scalar_tensor_tensor(out=dst[:, :, 1, 0:C], in0=bank(6 + u)[:, 0:4 * C].rearrange("p (a c) -> p a c", a=4),
                                             scalar=SCALE, in1=f32(dst[:, :, 0, 0:C]), op0=ALU.mult,
                                             op1=ALU.subtract).then_inc(mh_split, 1)

            part(0)
            with dve.Fori(1, PAIRS // 2) as i:
                part(i)
            for n in range(LEAD):
                quant_begin(n, n % 2)
                levels(n, range(LEVELS))
                quant_end(n, n % 2)

            def queries_lo(j, s, u):
                dve.wait_ge(q_hi, j + 1)
                dve.scalar_tensor_tensor(out=m["qe_lo"][:, s, :], in0=bank(6), scalar=m["bias_now"][:, u, s:s + 1],
                                         in1=f32(m["qe_hi"][:, s, :]), op0=ALU.add, op1=ALU.subtract).then_inc(q_split, 1)

            def normalise_1(k, tau):
                dve.wait_ge(exp_done, k + 1)
                dve.reciprocal(m["rinv"][:, tau:tau + 1], m["rowsum"][:, tau:tau + 1]).then_inc(rcp_done, 1)

            def normalise_2(k, tau):
                dve.wait_ge(rcp_done, k + 1)
                dve.tensor_scalar(m["prob"][:, tau, :], m["prob"][:, tau, :], m["rinv"][:, tau:tau + 1], None,
                                  ALU.mult).then_inc(prob_done, 1)

            def add_output(n):
                dve.wait_ge(o_psum, n + 1)
                if not (isinstance(n, int) and n == 0):
                    dve.wait_ge(o_added, n)
                o = m["osum"][:, bass.ds((n // PAIRS) * S, S)]
                dve.tensor_tensor(o, bank(6), o, ALU.add).then_inc(o_added, 1)

            def step(n, u, first=False, last=False):
                c = n + LEAD
                for tau in range(8):
                    k = 8 * n + tau
                    if tau == 0 and not (isinstance(n, int) and n < 2):
                        add_output(n - 2)
                    dve.wait_ge(score_psum, k + 1)
                    dve.tensor_reduce(m["negmax"][:, tau:tau + 1], bank(tau % 4), AX_X, ALU.max, negate=True).then_inc(max_done, 1)
                    if tau == 0:
                        queries_lo(2 * n + 1, 1, u)
                    if tau == 4 and not last:
                        queries_lo(2 * n + 2, 0, 1 - u)
                    started = not (first and tau == 0)
                    if started:
                        normalise_1(k - 1, (tau + 7) % 8)
                    if tau == 0:
                        quant_begin(c, u)
                        levels(c, range(0, 1))
                    else:
                        levels(c, range(2 * tau - 1, 2 * tau + 1))
                    if started:
                        normalise_2(k - 1, (tau + 7) % 8)
                quant_end(c, u)

            dve.wait_ge(rope_bias, 1)
            dve.wait_ge(osum_zero, 3)
            queries_lo(0, 0, 0)
            step(0, 0, first=True)
            step(1, 1)
            with dve.Fori(1, NP // 2 - 1) as i:
                for u in range(2):
                    step(2 * i + u, u)
            step(NP - 2, 0)
            step(NP - 1, 1, last=True)
            normalise_1(8 * NP - 1, 7)
            normalise_2(8 * NP - 1, 7)
            add_output(NP - 2)
            add_output(NP - 1)

            def part(i):
                for w, hi, lo in ((0, m["w1_hi"], m["w1_lo"]), (1, m["w2_hi"], m["w2_lo"])):
                    after(dve, wt_hi, 3 * i + w + 1)
                    split_lo(lo[:, :, bass.ds(i * P, P)], bank(w).rearrange("p (k q) -> p k q", k=HT),
                             hi[:, :, bass.ds(i * P, P)]).then_inc(wt_split, 1)
                after(dve, wt_hi, 3 * i + 3)
                at = bass.ds(i, 1)
                split_lo(m["w3_lo"][:, at, :].rearrange("p a (t q r) -> p (a t) r q", t=2, r=2),
                         bank(2).rearrange("p (t r q) -> p t r q", t=2, r=2),
                         m["w3_hi"][:, at, :].rearrange("p a (t q r) -> p (a t) r q", t=2, r=2)).then_inc(wt_split, 1)

            part(0)
            with dve.Fori(1, FT) as i:
                part(i)
            dve.memset(m["eps2"][:, :], EPS).then_inc(osum_zero, 1)

            dve.wait_ge(ffn_consts, 32)
            def part(b):
                def stats(src, which):
                    for t in range(TB):
                        dve.bn_stats(m["st2"][:, t, :], src(t)).then_inc(st_done, 1)
                    after(dve, st_done, 3 * TB * b + TB * (which + 1))
                    dve.memset(m["fence2"][:, :], 0.0)
                    for t in range(TB):
                        last = dve.bn_aggr(m["mv2"][:, t, :], m["st2"][:, t, :])
                    last.then_inc(var_done, 1)
                    after(dve, std_done, 3 * b + which + 1)
                    dve.reciprocal(m["rs2"][:, :], m["sd2"][:, :]).then_inc(inv_done, 1)
                    after(dve, inv_done, 3 * b + which + 1)

                def rows(name, t):
                    return m[name][:, t, :]

                after(dve, x1t_psum, TB * b)
                for t in range(TB):
                    after(dve, y_psum, TB * b + t + 1)
                    dve.tensor_tensor(rows("xn", t), bank(4 + t), m["bo"][:, :], ALU.add).then_inc(y_done, 1)
                after(dve, y_done, 3 * TB * b + TB)
                stats(lambda t: rows("xn", t), 0)
                after(dve, x1_in, 16 * b + 16)
                for t in range(TB):
                    dve.tensor_scalar(rows("xn", t), rows("xn", t), m["mv2"][:, t, 0:1], m["rs2"][:, t:t + 1],
                                      ALU.subtract, ALU.mult).then_inc(y_done, 1)
                for t in range(TB):
                    after(dve, y_done, 3 * TB * b + TB + t + 1)
                    last = dve.tensor_tensor(rows("x1", t), rows("x1", t), rows("xn", t), ALU.add)
                    last.then_inc(x1_done, 1)
                after(dve, x1_done, TB * b + TB)
                stats(lambda t: rows("x1", t), 1)
                for t in range(TB):
                    dve.tensor_scalar(rows("xn", t), rows("x1", t), m["mv2"][:, t, 0:1], m["rs2"][:, t:t + 1],
                                      ALU.subtract, ALU.mult).then_inc(xn_done, 1)
                for t in range(TB):
                    after(dve, x1t_hi_done, TB * b + t + 1)
                    split_lo(m["x1t_lo"][:, :, t * P:(t + 1) * P], bank(t).rearrange("p (k q) -> p k q", k=HT),
                             m["x1t_hi"][:, :, t * P:(t + 1) * P]).then_inc(x1t_split, 1)
                for i in range(FT):
                    after(dve, silu_done, FT * b + i + 1)
                    after(dve, up_psum, FT * b + i + 1)
                    after(dve, h_split, FT * b + i)
                    dve.tensor_tensor(m["hid"][:, :], bank(2 + i % 2), m["gate"][:, :], ALU.mult).then_inc(hid_done, 1)
                    after(dve, h_hi_done, FT * b + i + 1)
                    split_lo(m["h_lo"][:, i % 2, :], m["hid"][:, :], m["h_hi"][:, i % 2, :]).then_inc(h_split, 1)
                after(dve, down_psum, FT * b + FT)
                stats(lambda t: bank(4 + t), 2)
                for t in range(TB):
                    dve.tensor_scalar(rows("xn", t), bank(4 + t), m["mv2"][:, t, 0:1], m["rs2"][:, t:t + 1],
                                      ALU.subtract, ALU.mult).then_inc(y_done, 1)
                for t in range(TB):
                    after(dve, y_done, 3 * TB * b + 2 * TB + t + 1)
                    dve.tensor_tensor(rows("x1", t), rows("x1", t), rows("xn", t), ALU.add).then_inc(out_done, 1)

            part(0)
            with dve.Fori(1, B) as b:
                part(b)


_OUT = (B, S, H)


def kernel(L0_attn_hidden_size, L0_attn_Wq_c, L0_attn_bq_c, L0_attn_Wq_up, L0_attn_bq_up, L0_attn_Wkv_c,
           L0_attn_bkv_c, L0_attn_Wkv_up, L0_attn_bkv_up, L0_attn_Wo, L0_attn_bo, L0_ffn_w1, L0_ffn_w2, L0_ffn_w3):
    import concourse.bacc as bacc
    from concourse.bass_utils import run_bass_kernel_spmd

    def arr(a):
        return np.asarray(a)

    def rows_to_tiles(a):
        return a.reshape(-1, P, a.shape[1]).transpose(1, 0, 2)

    wq_c = arr(L0_attn_Wq_c).T
    wq_c = np.concatenate([wq_c, wq_c[:, P:]], axis=1)
    bq_c = arr(L0_attn_bq_c)
    wq_up = arr(L0_attn_Wq_up).reshape(NH, NOPE + ROPE, QL)
    bq_up = arr(L0_attn_bq_up).reshape(NH, NOPE + ROPE)
    nope = wq_up[:, :NOPE].transpose(1, 0, 2)
    ropeT = wq_up[:, NOPE:].transpose(2, 0, 1)
    wkv_up = arr(L0_attn_Wkv_up).reshape(NH, NOPE + VD, C)
    bkv_up = arr(L0_attn_bkv_up).reshape(NH, NOPE + VD)
    wv = wkv_up[:, NOPE:].reshape(PAIRS, 2, VD, C).transpose(1, 3, 0, 2).reshape(P, PAIRS * VD)
    w_ffn = np.zeros((P, QCOLS), np.float32)
    for at, w in ((W1_AT, arr(L0_ffn_w1)), (W2_AT, arr(L0_ffn_w2))):
        padded = np.zeros((FP, H), np.float32)
        padded[:F] = w
        w_ffn[:, at:at + FT * H] = rows_to_tiles(padded).reshape(P, FT * H)
    w3 = arr(L0_ffn_w3).reshape(2, P, 2 * F).transpose(1, 0, 2)
    w_ffn[:, W3_AT:W3_AT + W3_Q * F] = w3.reshape(P, W3_Q * F)

    ins = {
        "x": arr(L0_attn_hidden_size).reshape(TOK, H),
        "wq_cT": rows_to_tiles(wq_c),
        "bq_c": np.stack([bq_c[:P], np.concatenate([bq_c[P:], bq_c[P:]])], axis=1),
        "wkv_cT": rows_to_tiles(arr(L0_attn_Wkv_c).T),
        "bkv_c": arr(L0_attn_bkv_c)[:, None],
        "wq_nope": np.concatenate([nope, nope[:, :, P:]], axis=2),
        "wq_ropeT": np.stack([ropeT[:P], np.concatenate([ropeT[P:], ropeT[P:]])], axis=2),
        "bq_nope": bq_up[:, :NOPE].T,
        "bq_rope": bq_up[:, NOPE:].T,
        "wk_up": wkv_up[:, :NOPE].transpose(1, 0, 2),
        "wv_upT": wv,
        "bv_up": bkv_up[:, NOPE:].T,
        "woT": arr(L0_attn_Wo).T,
        "bo": arr(L0_attn_bo),
        "w_ffn": w_ffn,
        "ident": np.eye(P, dtype=np.float32),
    }
    nc = bacc.Bacc("TRN2", target_bir_lowering=False, num_devices=1)
    arrays, aps = {}, []
    for name, a in ins.items():
        a = np.ascontiguousarray(a)
        arrays[f"{name}_dram"] = a
        aps.append(nc.dram_tensor(f"{name}_dram", a.shape, mybir.dt.from_np(a.dtype), kind="ExternalInput").ap())
    out = nc.dram_tensor("out_dram", (TOK, H), F32, kind="ExternalOutput").ap()
    block_kernel(nc, *aps, out)
    r = run_bass_kernel_spmd(nc, [arrays], core_ids=[0])
    return r.results[0]["out_dram"].reshape(_OUT)
```
